# Optimizing a Trainium2 kernel written in Bass

```python
import numpy as np
import jax
import jax.numpy as jnp

def _softmax(x, axis=-1):
    return jax.nn.softmax(x, axis=axis)

def _gelu(x):
    return jax.nn.gelu(x, approximate=True)

def _silu(x):
    return jax.nn.silu(x)

def _sigmoid(x):
    return jax.nn.sigmoid(x)

def _layernorm(x, axis=-1, eps=1e-05):
    m = jnp.mean(x, axis=axis, keepdims=True)
    v = jnp.var(x, axis=axis, keepdims=True)
    return (x - m) / jnp.sqrt(v + eps)

def _scatter_add(tgt, idx, src, axis=0):
    return tgt.at[idx].add(src)

def _segment_sum(src, seg, n):
    return jax.ops.segment_sum(src, seg, n)
kernel_name = 'mk_adj_resnorm_d1_adj_r2_b193d0'

def setup_inputs(seed: int=0):
    np.random.seed(seed)
    _w = jnp.asarray

    def _rec_inputs():
        import jax
        import jax.numpy as jnp
        _gk = jax.random.key(seed)
        x = 7.22e-05 + 1 * jax.random.normal(jax.random.fold_in(_gk, 1), (128, 64, 512), jnp.float32)
        _w = (1.0 + jnp.arange(64, dtype=jnp.float32)) ** (-0.5)
        _w = _w / _w.mean()
        _pij = jnp.clip(0.125 * _w[:, None] * _w[None, :], 0.0, 1.0)
        _a = jax.random.uniform(jax.random.fold_in(_gk, 2), (128, 64, 64)) < _pij
        _a = jnp.logical_or(_a, jnp.eye(64, dtype=bool))
        adj = _a.astype(jnp.int32)
        return (x, adj)
    x, adj = _rec_inputs()

    def _L0_gnn_setup():
        import jax, jax.numpy as jnp
        import numpy as np
        import math
        D_MODEL = 512
        N_HEADS = 16
        D_HEAD = D_MODEL // N_HEADS
        B, S = (4, 1024)
        key = jax.random.key(seed)
        ks = jax.random.split(key, 10)
        x = jax.random.normal(ks[0], (B, S, D_MODEL), dtype=jnp.float32)
        mask = jax.random.randint(ks[1], (B, S, S), 0, 2, dtype=jnp.int32)
        eye = jnp.eye(S, dtype=jnp.int32)[None]
        mask = jnp.maximum(mask, eye)
        std = 1.0 / math.sqrt(D_MODEL)
        Wq = jax.random.normal(ks[2], (D_MODEL, D_MODEL), dtype=jnp.float32) * std
        Wk = jax.random.normal(ks[3], (D_MODEL, D_MODEL), dtype=jnp.float32) * std
        Wv = jax.random.normal(ks[4], (D_MODEL, D_MODEL), dtype=jnp.float32) * std
        Wo = jax.random.normal(ks[5], (D_MODEL, D_MODEL), dtype=jnp.float32) * std
        bq = jnp.zeros((D_MODEL,), dtype=jnp.float32)
        bk = jnp.zeros((D_MODEL,), dtype=jnp.float32)
        bv = jnp.zeros((D_MODEL,), dtype=jnp.float32)
        bo = jnp.zeros((D_MODEL,), dtype=jnp.float32)
        return {'x': x, 'mask': mask, 'Wq': Wq, 'bq': bq, 'Wk': Wk, 'bk': bk, 'Wv': Wv, 'bv': bv, 'Wo': Wo, 'bo': bo}
    _L0_gnn_all = _L0_gnn_setup()
    _L0_gnn_in = {k: v for k, v in _L0_gnn_all.items() if k in ('Wq', 'bq', 'Wk', 'bk', 'Wv', 'bv', 'Wo', 'bo')}
    del _L0_gnn_all
    return {'x': x, 'adj': adj, 'L0_gnn_Wq': _L0_gnn_in['Wq'], 'L0_gnn_bq': _L0_gnn_in['bq'], 'L0_gnn_Wk': _L0_gnn_in['Wk'], 'L0_gnn_bk': _L0_gnn_in['bk'], 'L0_gnn_Wv': _L0_gnn_in['Wv'], 'L0_gnn_bv': _L0_gnn_in['bv'], 'L0_gnn_Wo': _L0_gnn_in['Wo'], 'L0_gnn_bo': _L0_gnn_in['bo']}

def reference(x, adj, L0_gnn_Wq, L0_gnn_bq, L0_gnn_Wk, L0_gnn_bk, L0_gnn_Wv, L0_gnn_bv, L0_gnn_Wo, L0_gnn_bo):
    import jax
    import jax.numpy as jnp

    def _L0_gnn_ref(x, mask, Wq, bq, Wk, bk, Wv, bv, Wo, bo):
        import jax, jax.numpy as jnp
        import numpy as np
        import math
        D_MODEL = 512
        N_HEADS = 16
        D_HEAD = D_MODEL // N_HEADS
        B, S = (4, 1024)
        b, s, _ = x.shape
        scale = 1.0 / math.sqrt(D_HEAD)

        def heads(t):
            return t.reshape(b, s, N_HEADS, D_HEAD).transpose(0, 2, 1, 3)
        q = heads(x @ Wq + bq)
        k = heads(x @ Wk + bk)
        v = heads(x @ Wv + bv)
        scores = jnp.einsum('bhqd,bhkd->bhqk', q, k) * scale
        scores = jnp.where(mask[:, None] == 0, -jnp.inf, scores)
        attn = jax.nn.softmax(scores, axis=-1)
        out = jnp.einsum('bhqk,bhkd->bhqd', attn, v)
        out = out.transpose(0, 2, 1, 3).reshape(b, s, D_MODEL)
        return out @ Wo + bo
    x = _layernorm(x + _L0_gnn_ref(x, adj, L0_gnn_Wq, L0_gnn_bq, L0_gnn_Wk, L0_gnn_bk, L0_gnn_Wv, L0_gnn_bv, L0_gnn_Wo, L0_gnn_bo), axis=-1)
    return x

_drawn_inputs = setup_inputs


def setup_inputs(seed=0):
    import zlib

    import numpy as np

    out = dict(_drawn_inputs(seed))
    spreads = {'L0_gnn_bq': (0.0, 0.1),
     'L0_gnn_bk': (0.0, 0.1),
     'L0_gnn_bv': (0.0, 0.1),
     'L0_gnn_bo': (0.0, 0.1)}
    factors = {}
    for name, (base, spread) in spreads.items():
        noise = np.random.default_rng([zlib.crc32(name.encode()), seed]).standard_normal(out[name].shape)
        drawn = base * np.exp(spread * noise) if base else spread * noise
        out[name] = jnp.asarray(drawn.astype(out[name].dtype))
    for name, factor in factors.items():
        out[name] = (out[name] * factor).astype(out[name].dtype)
    return out
```

```python
import concourse.bass as bass
from concourse import mybir
from contextlib import ExitStack


def graph_attention_layernorm(nc, xT, x, adj, Wq, bq, Wk, bk, Wv, bv, Wo, bo, out):
    F32 = mybir.dt.float32
    F32R = mybir.dt.float32r
    I32 = mybir.dt.int32
    ALU = mybir.AluOpType
    ACT = mybir.ActivationFunctionType
    AX = mybir.AxisListType

    BATCHES, NODES, D = x.shape
    HEADS = 16
    DH = D // HEADS
    P = 128
    CH = D // P
    HC = P // DH
    PAIRS = BATCHES // 2
    GP = 4
    GN = GP * P
    HALF = HEADS // 2
    SCALE = float(DH) ** -0.5
    NEG = -1.0e30
    EPS = 1e-5

    UNIT_STEPS = PAIRS
    S_LAG, T_LAG, O_LAG = 4, 5, 6
    STEPS = PAIRS + O_LAG
    TURN = 8
    LOOP_END = UNIT_STEPS - TURN

    xT_v = xT.rearrange("(c p) n -> c p n", p=P)
    x_v = x.rearrange("b n d -> (b n) d")
    out_v = out.rearrange("b n d -> (b n) d")
    adj_v = adj.rearrange("(t b) q k -> (b q) t k", b=2)

    ctx = ExitStack()
    with ctx:
        def sb(name, shape, dt=F32):
            return ctx.enter_context(nc.sbuf_tensor(name, shape, dt))

        def pb(name, shape):
            return ctx.enter_context(nc.psum_tensor(name, shape, F32))

        def sem(name):
            return ctx.enter_context(nc.semaphore(name))

        w_hi = {n: sb(f"w{n}_hi", [P, CH, D], F32R) for n in "qkvo"}
        w_lo = {n: sb(f"w{n}_lo", [P, CH, D], F32R) for n in "qkvo"}
        x_raw = sb("x_raw", [P, CH, GN])
        x_hi = sb("x_hi", [P, 2, CH, GN + NODES], F32R)
        x_lo = sb("x_lo", [P, 2, CH, GN + NODES], F32R)
        qT = sb("qT", [P, 2, CH, GN])
        kT = sb("kT", [P, 2, CH, GN])
        v_sb = sb("v_sb", [P, 2, GP, D])
        k_diag = sb("k_diag", [P, 2, CH, 2, HC, NODES])
        scores = sb("scores", [P, 2, HEADS * NODES])
        probs = sb("probs", [P, HALF, 2, NODES])
        probsT = sb("probsT", [P, HALF, P])
        oT = sb("oT", [P, CH, 2, NODES])
        oT_hi = sb("oT_hi", [P, CH, P], F32R)
        oT_lo = sb("oT_lo", [P, CH, P], F32R)
        resid = sb("resid", [P, 2, D])
        bo_rows = sb("bo_rows", [P, D])
        bq_col = sb("bq_col", [P, CH])
        bk_col = sb("bk_col", [P, CH])
        bv_col = sb("bv_col", [P, CH])
        ident = sb("ident", [P, P])
        adj_sb = sb("adj_sb", [P, GP, NODES], I32)
        no_edge = sb("no_edge", [P, GP, NODES])
        row_max = sb("row_max", [P, 2, HEADS])
        row_sum = sb("row_sum", [P, 2, HEADS])
        row_inv = sb("row_inv", [P, 2, HEADS])
        stats = sb("stats", [P, nc.vector.BN_STATS_DIM])
        mean_var = sb("mean_var", [P, 2, 2])
        var_eps = sb("var_eps", [P, 1])
        rstd = sb("rstd", [P, 2])
        minus_half = sb("minus_half", [P, 1])

        ring = [pb(f"ring{i}", [P, D]) for i in range(2)]
        ps_scores = pb("ps_scores", [P, 2, HALF, NODES])
        ps_probsT = pb("ps_probsT", [P, HALF, P])
        ps_oT = pb("ps_oT", [P, 2, 2 * CH, NODES])

        weights_in = {n: sem(f"weights_in_{n}") for n in "qkvo"}
        biases_in = sem("biases_in")
        x_raw_in = [sem(f"x_raw_in{c}") for c in range(CH)]
        adj_in = sem("adj_in")
        resid_in = [sem(f"resid_in{i}") for i in range(2)]
        stored = [sem(f"stored{i}") for i in range(2)]
        consts_ready = sem("consts_ready")
        k_diag_zero = sem("k_diag_zero")
        w_hi_ready = sem("w_hi_ready")
        w_lo_ready = sem("w_lo_ready")
        x_hi_ready = sem("x_hi_ready")
        x_lo_ready = sem("x_lo_ready")
        unit_done = [sem(f"unit{n}_done") for n in "ABC"]
        unit_out = [sem(f"unit{n}_out") for n in "ABC"]
        scores_done = sem("scores_done")
        no_edge_ready = sem("no_edge_ready")
        scores_masked = sem("scores_masked")
        max_ready = sem("max_ready")
        shifted = sem("shifted")
        exp_ready = sem("exp_ready")
        sum_ready = sem("sum_ready")
        inv_ready = sem("inv_ready")
        probs_ready = sem("probs_ready")
        k_diag_ready = sem("k_diag_ready")
        transposed = sem("transposed")
        probsT_ready = sem("probsT_ready")
        attended = sem("attended")
        oT_ready = sem("oT_ready")
        oT_hi_ready = sem("oT_hi_ready")
        oT_lo_ready = sem("oT_lo_ready")
        projected = sem("projected")
        resid_biased = sem("resid_biased")
        y_ready = sem("y_ready")
        stats_ready = sem("stats_ready")
        mean_var_ready = sem("mean_var_ready")
        var_eps_ready = sem("var_eps_ready")
        rstd_ready = sem("rstd_ready")
        normed = sem("normed")

        waits_passed = {e: sem(f"waits_passed{i}") for i, e in enumerate((nc.gpsimd, nc.vector, nc.tensor))}

        block = ctx.enter_context(nc.Block())

        def steps(engine, step):
            for s in range(TURN):
                step(s, s)
            with engine.Fori(1, LOOP_END // TURN) as turn:
                for j in range(TURN):
                    step(turn * TURN + j, TURN + j)
            for s in range(LOOP_END, STEPS):
                step(s, s)

        def has_units(r):
            return r < UNIT_STEPS

        def has_pair(r, lag):
            return 0 <= r - lag < PAIRS

        def wait(engine, semaphore, value):
            if not isinstance(value, int) or value > 0:
                engine.wait_ge(semaphore, value)

        def wait_apart(engine, semaphore, value):
            wait(engine, semaphore, value)
            if not isinstance(value, int):
                engine.sem_inc(waits_passed[engine], 1)

        def units_of(r):
            for slot in range(3):
                u = 3 * (r % GP) + slot
                yield slot, "qkv"[u // 4], u % 4

        @block.sync
        def _(sp):
            def load_x(s, c):
                sp.dma_start(x_raw[:, c, :], xT_v[c, :, bass.ds((s - c) * P, GN)]).then_inc(x_raw_in[c], 16)

            sp.dma_start(x_raw[:, 0, :], xT_v[0, :, 0:GN]).then_inc(x_raw_in[0], 16)
            sp.dma_start(qT[:, 1], Wq.rearrange("(c p) n -> p c n", p=P)).then_inc(weights_in["q"], 16)
            for c in range(1, CH):
                sp.dma_start(x_raw[:, c, :], xT_v[c, :, 0:GN]).then_inc(x_raw_in[c], 16)
            sp.dma_start(kT[:, 1], Wk.rearrange("(c p) n -> p c n", p=P)).then_inc(weights_in["k"], 16)
            with nc.allow_non_contiguous_dma("three biases of 512 values, one per partition and chunk"):
                for col, b in ((bq_col, bq), (bk_col, bk), (bv_col, bv)):
                    sp.dma_start(col[:], b.rearrange("(c p) -> p c", p=P)).then_inc(biases_in, 16)
            sp.dma_start(v_sb[:, 1], Wv.rearrange("(c p) n -> p c n", p=P)).then_inc(weights_in["v"], 16)
            sp.dma_start(scores[:].rearrange("p a (c n) -> p (a c) n", n=D),
                         Wo.rearrange("(c p) n -> p c n", p=P)).then_inc(weights_in["o"], 16)
            sp.dma_start(bo_rows[:], bo.partition_broadcast(P)).then_inc(biases_in, 16)
            sp.dma_start(adj_sb[:], adj_v[:, 0:GP, :]).then_inc(adj_in, 16)
            for i in range(2):
                sp.dma_start(resid[:, i, :], x_v[i * P:(i + 1) * P, :]).then_inc(resid_in[i], 16)
            for c in range(CH):
                sp.wait_ge(x_lo_ready, c + 1)
                load_x(4 + c, c)

            def step(s, r):
                if r % GP == 0 and has_pair(r, S_LAG) and r < UNIT_STEPS:
                    sp.wait_ge(scores_masked, s - S_LAG + 1)
                    sp.dma_start(adj_sb[:], adj_v[:, bass.ds(s, GP), :]).then_inc(adj_in, 16)
                if r + 8 < UNIT_STEPS:
                    sp.wait_ge(x_lo_ready, s + 5)
                    load_x(s + 8, r % CH)
                if has_pair(r, O_LAG):
                    par = r % 2
                    sp.wait_ge(normed, s - O_LAG + 1)
                    sp.dma_start(out_v[bass.ds((s - O_LAG) * P, P), :],
                                 resid[:, par, :]).then_inc(stored[par], 16)
                    if has_pair(r + 2, O_LAG):
                        sp.wait_ge(stored[par], (s - O_LAG - par) * 8 + 16)
                        sp.dma_start(resid[:, par, :],
                                     x_v[bass.ds((s - O_LAG + 2) * P, P), :]).then_inc(resid_in[par], 16)

            steps(sp, step)
            for i in range(2):
                sp.wait_ge(stored[i], 16 * (PAIRS // 2))

        @block.gpsimd
        def _(pool):
            def split_x(s, r):
                c, par = r % CH, (r // CH) % 2
                wait_apart(pool, unit_done[2], s - c - 4)
                wait_apart(pool, x_raw_in[c], (s - c) * 4 + 16)
                nc.gpsimd.tensor_copy(x_hi[:, par, c, 0:GN], x_raw[:, c, :])
                nc.gpsimd.tensor_copy(x_hi[:, par, c, GN:], x_raw[:, c, 0:NODES]).then_inc(x_hi_ready, 1)
                pool.wait_ge(x_hi_ready, s + 1)
                nc.gpsimd.tensor_tensor(x_lo[:, par, c, 0:GN], x_raw[:, c, :],
                                        x_hi[:, par, c, 0:GN].bitcast(F32), ALU.subtract)
                nc.gpsimd.tensor_tensor(x_lo[:, par, c, GN:], x_raw[:, c, 0:NODES],
                                        x_hi[:, par, c, GN:].bitcast(F32), ALU.subtract).then_inc(x_lo_ready, 1)

            for c in range(CH):
                split_x(c, c)
            nc.gpsimd.memset(ident[:], 0.0).then_inc(consts_ready, 1)
            pool.wait_ge(consts_ready, 1)
            nc.gpsimd.affine_select(out=ident[:], in_=ident[:], compare_op=ALU.not_equal, fill=1.0, base=0,
                                    pattern=[[-1, P]], channel_multiplier=1).then_inc(consts_ready, 1)
            nc.gpsimd.memset(minus_half[:], -0.5).then_inc(consts_ready, 1)
            pool.wait_ge(biases_in, 64)
            pool.wait_ge(consts_ready, 3)

            def step(s, r):
                if has_pair(r, S_LAG):
                    par = r % 2
                    pool.wait_ge(max_ready, s - S_LAG + 1)
                    v = scores[:, par, :].rearrange("p (h k) -> p h k", k=NODES)
                    nc.gpsimd.tensor_tensor(v, v, row_max[:, par, :].unsqueeze(2).to_broadcast([P, HEADS, NODES]),
                                            ALU.subtract).then_inc(shifted, 1)
                if has_pair(r, O_LAG):
                    par = r % 2
                    pool.wait_ge(resid_in[par], (s - O_LAG - par) * 8 + 16)
                    nc.gpsimd.tensor_tensor(resid[:, par, :], resid[:, par, :], bo_rows[:],
                                            ALU.add).then_inc(resid_biased, 1)
                if r + 4 < UNIT_STEPS:
                    split_x(s + 4, r + 4)
                if has_pair(r, O_LAG):
                    par = r % 2
                    pool.wait_ge(var_eps_ready, s - O_LAG + 1)
                    nc.gpsimd.tensor_tensor(rstd[:, par:par + 1], var_eps[:], minus_half[:],
                                            ALU.pow).then_inc(rstd_ready, 1)
                if has_pair(r, S_LAG):
                    par = r % 2
                    pool.wait_ge(inv_ready, s - S_LAG + 1)
                    wait(pool, transposed, s - S_LAG)
                    nc.gpsimd.tensor_tensor(
                        probs[:].rearrange("p i t k -> p t i k"),
                        scores[:, par, :].rearrange("p (t i k) -> p t i k", t=2, k=NODES),
                        row_inv[:, par, :].rearrange("p (t i) -> p t i", t=2).unsqueeze(3)
                        .to_broadcast([P, 2, HALF, NODES]), ALU.mult).then_inc(probs_ready, 1)
                if has_pair(r, T_LAG):
                    wait_apart(pool, oT_ready, s - T_LAG + 1)
                    flat = oT[:].rearrange("p c b q -> p c (b q)")
                    nc.gpsimd.tensor_copy(oT_hi[:], flat).then_inc(oT_hi_ready, 1)
                    pool.wait_ge(oT_hi_ready, s - T_LAG + 1)
                    nc.gpsimd.tensor_tensor(oT_lo[:], flat, oT_hi[:].bitcast(F32),
                                            ALU.subtract).then_inc(oT_lo_ready, 1)

            steps(pool, step)

        staged = {"q": qT[:, 1], "k": kT[:, 1], "v": v_sb[:, 1],
                  "o": scores[:].rearrange("p a (c n) -> p (a c) n", n=D)}

        @block.scalar
        def _(act):
            for n in "qkvo":
                act.wait_ge(weights_in[n], 16)
                nc.scalar.copy(w_hi[n][:], staged[n]).then_inc(w_hi_ready, 1)
            act.wait_ge(biases_in, 64)
            act.wait_ge(w_lo_ready, 4)

            def unit_to_sbuf(s, r, slot):
                par = (r // GP) % 2
                _, kind, m = list(units_of(r))[slot]
                src = ring[0 if slot < 2 else 1][:]
                act.wait_ge(unit_done[slot], s + 1)
                if kind == "v":
                    ins = nc.scalar.copy(v_sb[:, par, m, :], src)
                else:
                    dst, bias = (qT, bq_col) if kind == "q" else (kT, bk_col)
                    ins = nc.scalar.activation(dst[:, par, m, :], src, ACT.Identity, bias=bias[:, m:m + 1])
                ins.then_inc(unit_out[slot], 1)

            def step(s, r):
                if 0 < r <= UNIT_STEPS:
                    unit_to_sbuf(s - 1, r - 1, 2)
                if has_units(r):
                    unit_to_sbuf(s, r, 0)
                if has_pair(r, T_LAG):
                    act.wait_ge(transposed, s - T_LAG + 1)
                    nc.scalar.copy(probsT[:], ps_probsT[:]).then_inc(probsT_ready, 1)
                if has_pair(r, S_LAG):
                    par = r % 2
                    act.wait_ge(shifted, s - S_LAG + 1)
                    nc.scalar.activation(scores[:, par, :], scores[:, par, :], ACT.Exp,
                                         scale=SCALE).then_inc(exp_ready, 1)
                if has_units(r):
                    unit_to_sbuf(s, r, 1)

            steps(act, step)

        @block.vector
        def _(dve):
            nc.vector.memset(k_diag[:], 0.0).then_inc(k_diag_zero, 1)
            for i, n in enumerate("qkvo"):
                dve.wait_ge(w_hi_ready, i + 1)
                nc.vector.tensor_tensor(w_lo[n][:], staged[n], w_hi[n][:].bitcast(F32),
                                        ALU.subtract).then_inc(w_lo_ready, 1)
            dve.wait_ge(biases_in, 64)
            dve.wait_ge(k_diag_zero, 1)

            def spread_keys(s, r):
                par, gpar, j = r % 2, ((r - S_LAG) // GP) % 2, r % GP
                if j == 0:
                    dve.wait_ge(unit_out[1], s - 1)
                wait(dve, scores_done, s - S_LAG - 1)
                for h in range(HC):
                    q = slice(h * DH, (h + 1) * DH)
                    last = nc.vector.tensor_copy(
                        k_diag[q, par, :, :, h, :],
                        kT[q, gpar, :, j * P:(j + 1) * P].rearrange("p c (b k) -> p c b k", b=2))
                last.then_inc(k_diag_ready, 1)

            def step(s, r):
                if has_pair(r, S_LAG):
                    par, j = r % 2, r % GP
                    if j == 0:
                        dve.wait_ge(adj_in, (s - S_LAG) * 4 + 16)
                        nc.vector.tensor_scalar(no_edge[:], adj_sb[:], 0, NEG, ALU.is_equal,
                                                ALU.mult).then_inc(no_edge_ready, 1)
                        dve.wait_ge(no_edge_ready, s // GP)
                    dve.wait_ge(scores_done, s - S_LAG + 1)
                    v = scores[:, par, :].rearrange("p (h k) -> p h k", k=NODES)
                    nc.vector.tensor_tensor(v, ps_scores[:].rearrange("p t i k -> p (t i) k"),
                                            no_edge[:, j:j + 1, :].to_broadcast([P, HEADS, NODES]),
                                            ALU.add).then_inc(scores_masked, 1)
                    dve.wait_ge(scores_masked, s - S_LAG + 1)
                    nc.vector.reduce_max(row_max[:, par, :], v, AX.X).then_inc(max_ready, 1)
                if has_pair(r + 1, S_LAG):
                    spread_keys(s + 1, r + 1)
                if has_pair(r, O_LAG):
                    par = r % 2
                    dve.wait_ge(projected, s - O_LAG + 1)
                    dve.wait_ge(resid_biased, s - O_LAG + 1)
                    nc.vector.tensor_tensor(resid[:, par, :], ring[1][:], resid[:, par, :],
                                            ALU.add).then_inc(y_ready, 1)
                    dve.wait_ge(y_ready, s - O_LAG + 1)
                    nc.vector.bn_stats(stats[:], resid[:, par, :]).then_inc(stats_ready, 1)
                    wait_apart(dve, stats_ready, s - O_LAG + 1)
                    nc.vector.bn_aggr(mean_var[:, par, :], stats[:]).then_inc(mean_var_ready, 1)
                    dve.wait_ge(mean_var_ready, s - O_LAG + 1)
                    nc.vector.tensor_scalar(var_eps[:], mean_var[:, par, 1:2], EPS, None,
                                            ALU.add).then_inc(var_eps_ready, 1)
                if has_pair(r, S_LAG):
                    par = r % 2
                    dve.wait_ge(exp_ready, s - S_LAG + 1)
                    nc.vector.reduce_sum(row_sum[:, par, :],
                                         scores[:, par, :].rearrange("p (h k) -> p h k", k=NODES),
                                         AX.X).then_inc(sum_ready, 1)
                    dve.wait_ge(sum_ready, s - S_LAG + 1)
                    nc.vector.reciprocal(row_inv[:, par, :], row_sum[:, par, :]).then_inc(inv_ready, 1)
                if has_pair(r, T_LAG):
                    dve.wait_ge(attended, s - T_LAG + 1)
                    nc.vector.tensor_tensor(
                        oT[:, 0:2], ps_oT[:, :, 0:2, :].rearrange("p b c q -> p c b q"),
                        bv_col[:, 0:2].unsqueeze(2).unsqueeze(3).to_broadcast([P, 2, 2, NODES]), ALU.add)
                    for b in range(2):
                        last = nc.vector.tensor_tensor(
                            oT[:, 2:4, b, :], ps_oT[:, 1 - b, 2:4, :],
                            bv_col[:, 2:4].unsqueeze(2).to_broadcast([P, 2, NODES]), ALU.add)
                    last.then_inc(oT_ready, 1)
                if has_pair(r, O_LAG):
                    par = r % 2
                    dve.wait_ge(rstd_ready, s - O_LAG + 1)
                    nc.vector.tensor_scalar(resid[:, par, :], resid[:, par, :], mean_var[:, par, 0:1],
                                            rstd[:, par:par + 1], ALU.subtract, ALU.mult).then_inc(normed, 1)

            steps(dve, step)

        @block.tensor
        def _(pe):
            def split_matmuls(dst, lhs, rhs):
                for c in range(CH):
                    (l_hi, l_lo), (r_hi, r_lo) = lhs(c), rhs(c)
                    nc.tensor.matmul(dst, l_hi, r_hi, start=(c == 0), stop=False)
                    nc.tensor.matmul(dst, l_hi, r_lo, start=False, stop=False)
                    last = nc.tensor.matmul(dst, l_lo, r_hi, start=False, stop=(c == CH - 1))
                return last

            def unit(s, r, slot):
                par = (r // GP) % 2
                _, kind, m = list(units_of(r))[slot]
                dst = ring[0 if slot < 2 else 1]
                if kind in "qk":
                    cols = slice(m * P, (m + 1) * P)
                    last = split_matmuls(
                        dst[:], lambda c: (w_hi[kind][:, c, cols], w_lo[kind][:, c, cols]),
                        lambda c: (x_hi[:, par, c, 0:GN], x_lo[:, par, c, 0:GN]))
                else:
                    for half in range(2):
                        rows = slice(m * P + half * NODES, m * P + half * NODES + P)
                        cols = slice(half * (D // 2), (half + 1) * (D // 2))
                        last = split_matmuls(
                            dst[:, cols], lambda c: (x_hi[:, par, c, rows], x_lo[:, par, c, rows]),
                            lambda c: (w_hi["v"][:, c, cols], w_lo["v"][:, c, cols]))
                last.then_inc(unit_done[slot], 1)

            def step(s, r):
                if has_pair(r, S_LAG):
                    par, gpar, j = r % 2, ((r - S_LAG) // GP) % 2, r % GP
                    pe.wait_ge(k_diag_ready, s - S_LAG + 1)
                    wait(pe, scores_masked, s - S_LAG)
                    for c in range(CH):
                        for b in range(2):
                            n0 = j * P + b * NODES
                            last = nc.tensor.matmul(
                                ps_scores[b * NODES:(b + 1) * NODES, (c // 2) ^ b, (c % 2) * HC:(c % 2 + 1) * HC, :],
                                qT[:, gpar, c, n0:n0 + NODES],
                                k_diag[:, par, c, b, :, :], start=True, stop=True)
                    last.then_inc(scores_done, 1)
                if has_units(r):
                    if r == 0:
                        pe.wait_ge(w_lo_ready, 1)
                    if r == 1:
                        pe.wait_ge(w_lo_ready, 2)
                    if r % GP == 0:
                        pe.wait_ge(x_lo_ready, s + 4)
                    wait(pe, unit_out[1], s)
                    unit(s, r, 0)
                if has_pair(r, T_LAG):
                    if r == T_LAG:
                        pe.wait_ge(consts_ready, 2)
                    pe.wait_ge(probs_ready, s - T_LAG + 1)
                    wait(pe, probsT_ready, s - T_LAG)
                    for i in range(HALF):
                        last = nc.tensor.transpose(ps_probsT[:, i, :],
                                                   probs[:, i, :, :].rearrange("p t k -> p (t k)"), ident[:])
                    last.then_inc(transposed, 1)
                if has_pair(r, O_LAG):
                    pe.wait_ge(oT_lo_ready, s - O_LAG + 1)
                    if r <= UNIT_STEPS:
                        pe.wait_ge(unit_out[2], s)
                    else:
                        pe.wait_ge(y_ready, s - O_LAG)
                    split_matmuls(ring[1][:], lambda c: (oT_hi[:, c, :], oT_lo[:, c, :]),
                                  lambda c: (w_hi["o"][:, c, :], w_lo["o"][:, c, :])).then_inc(projected, 1)
                if has_pair(r, T_LAG):
                    gpar, j = ((r - T_LAG) // GP) % 2, (r - T_LAG) % GP
                    wait_apart(pe, probsT_ready, s - T_LAG + 1)
                    wait_apart(pe, oT_ready, s - T_LAG)
                    for half in range(2):
                        for b in range(2):
                            row = half ^ b
                            window = j if half == 0 or b == 1 else (j - 1) % GP
                            k0 = row * NODES
                            for i in range(HALF):
                                h = half * HALF + i
                                quad, c = h % HC, h // HC
                                last = nc.tensor.matmul(
                                    ps_oT[quad * DH:(quad + 1) * DH, row, c, :],
                                    v_sb[k0:k0 + NODES, gpar, window, h * DH:(h + 1) * DH],
                                    probsT[k0:k0 + NODES, i, b * NODES:(b + 1) * NODES],
                                    start=True, stop=True)
                    last.then_inc(attended, 1)
                if has_units(r):
                    if r == 2:
                        pe.wait_ge(w_lo_ready, 3)
                    pe.wait_ge(unit_out[0], s + 1)
                    unit(s, r, 1)
                    if has_pair(r, O_LAG):
                        pe.wait_ge(y_ready, s - O_LAG + 1)
                    else:
                        wait(pe, unit_out[2], s)
                    unit(s, r, 2)

            steps(pe, step)


_INS = ["x", "adj", "L0_gnn_Wq", "L0_gnn_bq", "L0_gnn_Wk", "L0_gnn_bk",
        "L0_gnn_Wv", "L0_gnn_bv", "L0_gnn_Wo", "L0_gnn_bo"]


def kernel(**inputs):
    import numpy as np
    import concourse.bacc as bacc
    from concourse.bass_utils import run_bass_kernel_spmd

    nc = bacc.Bacc("TRN2", target_bir_lowering=False, num_devices=1)
    x = np.asarray(inputs["x"])
    arrays = {"in_xT": np.ascontiguousarray(x.reshape(-1, x.shape[-1]).T)}
    for name in _INS:
        arrays[f"in_{name}"] = np.ascontiguousarray(inputs[name])
    aps = [nc.dram_tensor(k, a.shape, mybir.dt.from_np(a.dtype), kind="ExternalInput").ap()
           for k, a in arrays.items()]
    out = nc.dram_tensor("out", x.shape, mybir.dt.float32, kind="ExternalOutput").ap()
    graph_attention_layernorm(nc, *aps, out)
    r = run_bass_kernel_spmd(nc, [arrays], core_ids=[0])
    return r.results[0]["out"]
```

```python
import concourse.bass as bass
from concourse import mybir
from contextlib import ExitStack


def graph_attention_layernorm(nc, xT, x, adj, Wq, bq, Wk, bk, Wv, bv, Wo, bo, out):
    F32 = mybir.dt.float32
    F32R = mybir.dt.float32r
    I32 = mybir.dt.int32
    ALU = mybir.AluOpType
    ACT = mybir.ActivationFunctionType
    AX = mybir.AxisListType

    BATCHES, NODES, D = x.shape
    HEADS = 16
    DH = D // HEADS
    P = 128
    CH = D // P
    HC = P // DH
    PAIRS = BATCHES // 2
    GP = 4
    GN = GP * P
    SCALE = float(DH) ** -0.5
    NEG = -1.0e30
    EPS = 1e-5

    V_LAG, T_LAG, O_LAG = 4, 5, 6
    AHEAD = 4
    STEPS = PAIRS + O_LAG
    TURN = 8
    LOOP_END = PAIRS - TURN

    xT_v = xT.rearrange("(c p) n -> p c n", p=P)
    x_v = x.rearrange("b n d -> (b n) d")
    out_v = out.rearrange("b n d -> (b n) d")
    adj_v = adj.rearrange("(t b) q k -> (b q) t k", b=2)

    ctx = ExitStack()
    with ctx:
        def sb(name, shape, dt=F32):
            return ctx.enter_context(nc.sbuf_tensor(name, shape, dt))

        def pb(name, shape):
            return ctx.enter_context(nc.psum_tensor(name, shape, F32))

        def sem(name):
            return ctx.enter_context(nc.semaphore(name))

        w_hi = {n: sb(f"w{n}_hi", [P, CH, D], F32R) for n in "qkvo"}
        w_lo = {n: sb(f"w{n}_lo", [P, CH, D], F32R) for n in "qkvo"}
        w_stage = sb("w_stage", [P, 2, CH, D])
        x_raw = sb("x_raw", [P, 2, CH, P])
        x_hi = sb("x_hi", [P, 2, CH, GN], F32R)
        x_lo = sb("x_lo", [P, 2, CH, GN], F32R)
        qT = sb("qT", [P, 2, CH, GN])
        kT = sb("kT", [P, 2, CH, GN])
        v_sb = sb("v_sb", [P, 2, D])
        k_diag = sb("k_diag", [P, 2, CH, 2, HC, NODES])
        scores = sb("scores", [P, 2, HEADS, NODES])
        probsT = sb("probsT", [P, HEADS, NODES])
        oT = sb("oT", [P, CH, 2, NODES])
        oT_hi = sb("oT_hi", [P, CH, P], F32R)
        oT_lo = sb("oT_lo", [P, CH, P], F32R)
        resid = sb("resid", [P, 2, D])
        bo_rows = sb("bo_rows", [P, D])
        bq_col = sb("bq_col", [P, CH])
        bk_col = sb("bk_col", [P, CH])
        bv_col = sb("bv_col", [P, CH])
        adj_sb = sb("adj_sb", [P, GP, NODES], I32)
        no_edge = sb("no_edge", [P, GP, NODES])
        row_max = sb("row_max", [P, 2, HEADS])
        row_sum = sb("row_sum", [P, 2, HEADS])
        row_inv = sb("row_inv", [P, 2, HEADS])
        stats = sb("stats", [P, nc.vector.BN_STATS_DIM])
        mean_var = sb("mean_var", [P, 2, 2])
        var_eps = sb("var_eps", [P, 1])
        rstd = sb("rstd", [P, 2])
        minus_half = sb("minus_half", [P, 1])

        ps_v = pb("ps_v", [P, D])
        ps_qk = [pb(f"ps_qk{i}", [P, GN]) for i in range(2)]
        ps_out = pb("ps_out", [P, D])
        ps_scores = pb("ps_scores", [P, HEADS, NODES])
        ps_oT = pb("ps_oT", [P, 2, 2 * CH, NODES])

        x_first_in = [sem(f"x_first_in{c}") for c in range(CH)]
        wq_in = [sem(f"wq_in{c}") for c in range(CH)]
        weights_in = {n: sem(f"weights_in_{n}") for n in "kvo"}
        biases_in = sem("biases_in")
        bo_in = sem("bo_in")
        x_raw_in = [sem(f"x_raw_in{i}") for i in range(2)]
        adj_in = sem("adj_in")
        resid_in = [sem(f"resid_in{i}") for i in range(2)]
        stored = [sem(f"stored{i}") for i in range(2)]
        half_ready = sem("half_ready")
        k_diag_zero = sem("k_diag_zero")
        w_hi_ready = sem("w_hi_ready")
        w_vo_hi_ready = sem("w_vo_hi_ready")
        w_lo_ready = sem("w_lo_ready")
        x_hi_ready = sem("x_hi_ready")
        x_lo_ready = sem("x_lo_ready")
        v_done = sem("v_done")
        v_ready = sem("v_ready")
        qk_done = [sem(f"qk{i}_done") for i in range(2)]
        qk_out = [sem(f"qk{i}_out") for i in range(2)]
        k_diag_ready = sem("k_diag_ready")
        scores_done = sem("scores_done")
        no_edge_ready = sem("no_edge_ready")
        scores_masked = sem("scores_masked")
        max_ready = sem("max_ready")
        shifted = sem("shifted")
        exp_ready = sem("exp_ready")
        sum_ready = sem("sum_ready")
        inv_ready = sem("inv_ready")
        probs_ready = sem("probs_ready")
        probsT_ready = sem("probsT_ready")
        attended = sem("attended")
        oT_ready = sem("oT_ready")
        oT_hi_ready = sem("oT_hi_ready")
        oT_lo_ready = sem("oT_lo_ready")
        projected = sem("projected")
        resid_biased = sem("resid_biased")
        y_ready = sem("y_ready")
        stats_ready = sem("stats_ready")
        mean_var_ready = sem("mean_var_ready")
        var_eps_ready = sem("var_eps_ready")
        rstd_ready = sem("rstd_ready")
        normed = sem("normed")
        waits_passed = {e: sem(f"waits_passed{i}") for i, e in enumerate((nc.gpsimd, nc.vector, nc.tensor))}

        block = ctx.enter_context(nc.Block())

        def steps(engine, step):
            for s in range(TURN):
                step(s, s)
            with engine.Fori(1, LOOP_END // TURN) as turn:
                for j in range(TURN):
                    step(turn * TURN + j, TURN + j)
            for s in range(LOOP_END, STEPS):
                step(s, s)

        def has_pair(r, lag):
            return 0 <= r - lag < PAIRS

        def wait(engine, semaphore, value):
            if not isinstance(value, int) or value > 0:
                engine.wait_ge(semaphore, value)

        def wait_apart(engine, semaphore, value):
            wait(engine, semaphore, value)
            if not isinstance(value, int):
                engine.sem_inc(waits_passed[engine], 1)

        def qk_chunk(r, i):
            u = 2 * (r % GP) + i
            return "qk"[u // CH], u % CH

        x_first = scores[:].rearrange("p a h k -> p (a h k)").rearrange("p (c n) -> p c n", n=GN)
        staged = {"q": qT[:, 1], "k": kT[:, 1], "v": w_stage[:, 0], "o": w_stage[:, 1]}

        @block.sync
        def _(sp):
            def load_x(s, r):
                sp.dma_start(x_raw[:, r % 2], xT_v[:, :, bass.ds(s * P, P)]).then_inc(x_raw_in[r % 2], 16)

            for c in range(CH):
                sp.dma_start(x_first[:, c, :], xT_v[:, c, 0:GN]).then_inc(x_first_in[c], 16)
                sp.dma_start(staged["q"][:, c, :], Wq[c * P:(c + 1) * P, :]).then_inc(wq_in[c], 16)
            sp.dma_start(staged["k"], Wk.rearrange("(c p) n -> p c n", p=P)).then_inc(weights_in["k"], 16)
            with nc.allow_non_contiguous_dma("three biases of 512 values, one per partition and chunk"):
                for col, b in ((bq_col, bq), (bk_col, bk), (bv_col, bv)):
                    sp.dma_start(col[:], b.rearrange("(c p) -> p c", p=P)).then_inc(biases_in, 16)
            for n, w in (("v", Wv), ("o", Wo)):
                sp.dma_start(staged[n], w.rearrange("(c p) n -> p c n", p=P)).then_inc(weights_in[n], 16)
            for t in range(AHEAD, AHEAD + 2):
                load_x(t, t)
            sp.dma_start(adj_sb[:], adj_v[:, 0:GP, :]).then_inc(adj_in, 16)
            sp.dma_start(bo_rows[:], bo.partition_broadcast(P)).then_inc(bo_in, 16)
            for i in range(2):
                sp.dma_start(resid[:, i, :], x_v[i * P:(i + 1) * P, :]).then_inc(resid_in[i], 16)

            def step(s, r):
                if r % GP == 0 and has_pair(r, V_LAG) and r < PAIRS:
                    sp.wait_ge(scores_masked, s - V_LAG + 1)
                    sp.dma_start(adj_sb[:], adj_v[:, bass.ds(s, GP), :]).then_inc(adj_in, 16)
                if r + AHEAD + 2 < PAIRS:
                    sp.wait_ge(x_lo_ready, s + AHEAD + 1)
                    load_x(s + AHEAD + 2, r)
                if has_pair(r, O_LAG):
                    par = r % 2
                    sp.wait_ge(normed, s - O_LAG + 1)
                    sp.dma_start(out_v[bass.ds((s - O_LAG) * P, P), :],
                                 resid[:, par, :]).then_inc(stored[par], 16)
                    if has_pair(r + 2, O_LAG):
                        sp.wait_ge(stored[par], (s - O_LAG - par) * 8 + 16)
                        sp.dma_start(resid[:, par, :],
                                     x_v[bass.ds((s - O_LAG + 2) * P, P), :]).then_inc(resid_in[par], 16)

            steps(sp, step)
            for i in range(2):
                sp.wait_ge(stored[i], 16 * (PAIRS // 2))

        @block.gpsimd
        def _(pool):
            nc.gpsimd.memset(minus_half[:], -0.5).then_inc(half_ready, 1)
            for c in range(CH):
                pool.wait_ge(x_hi_ready, c + 1)
                nc.gpsimd.tensor_tensor(x_lo[:, 0, c, :], x_first[:, c, :], x_hi[:, 0, c, :].bitcast(F32),
                                        ALU.subtract).then_inc(x_lo_ready, 1)
            nc.gpsimd.memset(k_diag[:], 0.0).then_inc(k_diag_zero, 1)
            pool.wait_ge(bo_in, 16)
            pool.wait_ge(half_ready, 1)

            def step(s, r):
                par = r % 2
                if r + AHEAD < PAIRS:
                    gpar, n = (r // GP + 1) % 2, slice(r % GP * P, (r % GP + 1) * P)
                    pool.wait_ge(x_hi_ready, s + AHEAD + 1)
                    nc.gpsimd.tensor_tensor(x_lo[:, gpar, :, n], x_raw[:, par], x_hi[:, gpar, :, n].bitcast(F32),
                                            ALU.subtract).then_inc(x_lo_ready, 1)
                if has_pair(r, O_LAG):
                    pool.wait_ge(resid_in[par], (s - O_LAG - par) * 8 + 16)
                    nc.gpsimd.tensor_tensor(resid[:, par, :], resid[:, par, :], bo_rows[:],
                                            ALU.add).then_inc(resid_biased, 1)
                if has_pair(r, V_LAG):
                    pool.wait_ge(max_ready, s - V_LAG + 1)
                    nc.gpsimd.tensor_tensor(scores[:, par], scores[:, par],
                                            row_max[:, par, :].unsqueeze(2).to_broadcast([P, HEADS, NODES]),
                                            ALU.subtract).then_inc(shifted, 1)
                if has_pair(r, O_LAG):
                    pool.wait_ge(var_eps_ready, s - O_LAG + 1)
                    nc.gpsimd.tensor_tensor(rstd[:, par:par + 1], var_eps[:], minus_half[:],
                                            ALU.pow).then_inc(rstd_ready, 1)
                if has_pair(r, T_LAG):
                    pool.wait_ge(oT_hi_ready, s - T_LAG + 1)
                    nc.gpsimd.tensor_tensor(oT_lo[:], oT[:].rearrange("p c b q -> p c (b q)"),
                                            oT_hi[:].bitcast(F32), ALU.subtract).then_inc(oT_lo_ready, 1)
                if has_pair(r, V_LAG):
                    pool.wait_ge(inv_ready, s - V_LAG + 1)
                    nc.gpsimd.tensor_tensor(scores[:, par], scores[:, par],
                                            row_inv[:, par, :].unsqueeze(2).to_broadcast([P, HEADS, NODES]),
                                            ALU.mult).then_inc(probs_ready, 1)

            steps(pool, step)

        @block.scalar
        def _(act):
            for c in range(CH):
                act.wait_ge(x_first_in[c], 16)
                nc.scalar.copy(x_hi[:, 0, c, :], x_first[:, c, :]).then_inc(x_hi_ready, 1)
                act.wait_ge(wq_in[c], 16)
                nc.scalar.copy(w_hi["q"][:, c, :], staged["q"][:, c, :]).then_inc(w_hi_ready, 1)
            act.wait_ge(weights_in["k"], 16)
            for c in range(CH):
                nc.scalar.copy(w_hi["k"][:, c, :], staged["k"][:, c, :]).then_inc(w_hi_ready, 1)
            act.wait_ge(biases_in, 48)

            def qk_to_sbuf(s, r, i):
                gpar = (r // GP) % 2
                kind, m = qk_chunk(r, i)
                dst, bias = (qT, bq_col) if kind == "q" else (kT, bk_col)
                act.wait_ge(qk_done[i], s + 1)
                nc.scalar.activation(dst[:, gpar, m, :], ps_qk[i][:], ACT.Identity,
                                     bias=bias[:, m:m + 1]).then_inc(qk_out[i], 1)

            def spread_keys(s, r):
                par, gpar, j = r % 2, ((r - V_LAG) // GP) % 2, r % GP
                if j == 0:
                    act.wait_ge(qk_out[1], s)
                if r == V_LAG:
                    act.wait_ge(k_diag_zero, 1)
                wait(act, scores_done, s - V_LAG - 1)
                for h in range(HC):
                    q = slice(h * DH, (h + 1) * DH)
                    last = nc.scalar.copy(
                        k_diag[q, par, :, :, h, :],
                        kT[q, gpar, :, j * P:(j + 1) * P].rearrange("p c (b k) -> p c b k", b=2))
                last.then_inc(k_diag_ready, 1)

            def step(s, r):
                par = r % 2
                if 0 < r <= PAIRS:
                    qk_to_sbuf(s - 1, r - 1, 1)
                if has_pair(r, V_LAG) and r % GP == 0:
                    spread_keys(s, r)
                if has_pair(r, V_LAG):
                    act.wait_ge(v_done, s - V_LAG + 1)
                    nc.scalar.copy(v_sb[:, par, :], ps_v[:]).then_inc(v_ready, 1)
                if r + AHEAD < PAIRS:
                    gpar, n = (r // GP + 1) % 2, slice(r % GP * P, (r % GP + 1) * P)
                    act.wait_ge(x_raw_in[par], (s - par) * 8 + 16)
                    nc.scalar.copy(x_hi[:, gpar, :, n], x_raw[:, par]).then_inc(x_hi_ready, 1)
                if has_pair(r + 1, V_LAG) and (r + 1) % GP != 0:
                    spread_keys(s + 1, r + 1)
                if has_pair(r, V_LAG):
                    act.wait_ge(shifted, s - V_LAG + 1)
                    nc.scalar.activation(scores[:, par], scores[:, par], ACT.Exp, scale=SCALE).then_inc(exp_ready, 1)
                if has_pair(r, T_LAG):
                    act.wait_ge(oT_ready, s - T_LAG + 1)
                    nc.scalar.copy(oT_hi[:], oT[:].rearrange("p c b q -> p c (b q)")).then_inc(oT_hi_ready, 1)
                if r < PAIRS:
                    qk_to_sbuf(s, r, 0)

            steps(act, step)

        @block.vector
        def _(dve):
            for i, n in enumerate("qkvo"):
                if n == "k":
                    dve.wait_ge(weights_in["k"], 16)
                if n in "vo":
                    dve.wait_ge(weights_in[n], 16)
                    for c in range(CH):
                        nc.vector.tensor_copy(w_hi[n][:, c, :], staged[n][:, c, :]).then_inc(w_vo_hi_ready, 1)
                for c in range(CH):
                    if n in "qk":
                        dve.wait_ge(w_hi_ready, CH * i + c + 1)
                    else:
                        dve.wait_ge(w_vo_hi_ready, CH * (i - 2) + c + 1)
                    nc.vector.tensor_tensor(w_lo[n][:, c, :], staged[n][:, c, :], w_hi[n][:, c, :].bitcast(F32),
                                            ALU.subtract).then_inc(w_lo_ready, 1)
            dve.wait_ge(biases_in, 48)

            def step(s, r):
                par = r % 2
                if has_pair(r, T_LAG):
                    dve.wait_ge(probs_ready, s - T_LAG + 1)
                    for b in range(2):
                        for qh in range(2):
                            for kh in range(2):
                                src, dst = b * NODES + qh * DH, b * NODES + kh * DH
                                last = nc.vector.transpose(
                                    probsT[dst:dst + DH, :, qh * DH:(qh + 1) * DH],
                                    scores[src:src + DH, 1 - par, :, kh * DH:(kh + 1) * DH])
                    last.then_inc(probsT_ready, 1)
                if has_pair(r, V_LAG):
                    j = r % GP
                    if j == 0:
                        dve.wait_ge(adj_in, (s - V_LAG) * 4 + 16)
                        nc.vector.tensor_scalar(no_edge[:], adj_sb[:], 0, NEG, ALU.is_equal,
                                                ALU.mult).then_inc(no_edge_ready, 1)
                        dve.wait_ge(no_edge_ready, s // GP)
                    dve.wait_ge(scores_done, s - V_LAG + 1)
                    nc.vector.tensor_tensor(scores[:, par], ps_scores[:],
                                            no_edge[:, j:j + 1, :].to_broadcast([P, HEADS, NODES]),
                                            ALU.add).then_inc(scores_masked, 1)
                    dve.wait_ge(scores_masked, s - V_LAG + 1)
                    nc.vector.reduce_max(row_max[:, par, :], scores[:, par], AX.X).then_inc(max_ready, 1)
                if has_pair(r, O_LAG):
                    dve.wait_ge(projected, s - O_LAG + 1)
                    dve.wait_ge(resid_biased, s - O_LAG + 1)
                    nc.vector.tensor_tensor(resid[:, par, :], ps_out[:], resid[:, par, :],
                                            ALU.add).then_inc(y_ready, 1)
                    dve.wait_ge(y_ready, s - O_LAG + 1)
                    nc.vector.bn_stats(stats[:], resid[:, par, :]).then_inc(stats_ready, 1)
                    wait_apart(dve, stats_ready, s - O_LAG + 1)
                    nc.vector.bn_aggr(mean_var[:, par, :], stats[:]).then_inc(mean_var_ready, 1)
                    dve.wait_ge(mean_var_ready, s - O_LAG + 1)
                    nc.vector.tensor_scalar(var_eps[:], mean_var[:, par, 1:2], EPS, None,
                                            ALU.add).then_inc(var_eps_ready, 1)
                if has_pair(r, T_LAG):
                    dve.wait_ge(attended, s - T_LAG + 1)
                    for b in range(2):
                        last = nc.vector.tensor_tensor(
                            oT[:, :, b, :], ps_oT[:, b, 0:CH, :],
                            bv_col[:].unsqueeze(2).to_broadcast([P, CH, NODES]), ALU.add)
                    last.then_inc(oT_ready, 1)
                if has_pair(r, V_LAG):
                    dve.wait_ge(exp_ready, s - V_LAG + 1)
                    nc.vector.reduce_sum(row_sum[:, par, :], scores[:, par], AX.X).then_inc(sum_ready, 1)
                    dve.wait_ge(sum_ready, s - V_LAG + 1)
                    nc.vector.reciprocal(row_inv[:, par, :], row_sum[:, par, :]).then_inc(inv_ready, 1)
                if has_pair(r, O_LAG):
                    dve.wait_ge(rstd_ready, s - O_LAG + 1)
                    nc.vector.tensor_scalar(resid[:, par, :], resid[:, par, :], mean_var[:, par, 0:1],
                                            rstd[:, par:par + 1], ALU.subtract, ALU.mult).then_inc(normed, 1)

            steps(dve, step)

        @block.tensor
        def _(pe):
            def split_matmuls(dst, lhs, rhs, ready=lambda c: None):
                for c in range(CH):
                    ready(c)
                    (l_hi, l_lo), (r_hi, r_lo) = lhs(c), rhs(c)
                    nc.tensor.matmul(dst, l_hi, r_hi, start=(c == 0), stop=False)
                    nc.tensor.matmul(dst, l_hi, r_lo, start=False, stop=False)
                    last = nc.tensor.matmul(dst, l_lo, r_hi, start=False, stop=(c == CH - 1))
                return last

            def project_qk(s, r, i):
                gpar = (r // GP) % 2
                kind, m = qk_chunk(r, i)
                cols = slice(m * P, (m + 1) * P)

                def ready(c):
                    if kind == "q" and r < GP:
                        pe.wait_ge(w_lo_ready, c + 1)
                        pe.wait_ge(x_lo_ready, c + 1)
                    if kind == "k" and r < GP:
                        pe.wait_ge(w_lo_ready, CH + c + 1)

                split_matmuls(ps_qk[i][:], lambda c: (w_hi[kind][:, c, cols], w_lo[kind][:, c, cols]),
                              lambda c: (x_hi[:, gpar, c, :], x_lo[:, gpar, c, :]), ready).then_inc(qk_done[i], 1)

            def step(s, r):
                par = r % 2
                gpar, j = ((r - V_LAG) // GP) % 2, r % GP
                if has_pair(r, V_LAG):
                    if r == V_LAG:
                        pe.wait_ge(w_lo_ready, 3 * CH)
                    wait(pe, v_ready, s - V_LAG)
                    n = slice(j * P, (j + 1) * P)
                    split_matmuls(ps_v[:], lambda c: (x_hi[:, gpar, c, n], x_lo[:, gpar, c, n]),
                                  lambda c: (w_hi["v"][:, c, :], w_lo["v"][:, c, :])).then_inc(v_done, 1)
                    pe.wait_ge(k_diag_ready, s - V_LAG + 1)
                    wait(pe, scores_masked, s - V_LAG)
                    for c in range(CH):
                        for b in range(2):
                            n0 = j * P + b * NODES
                            last = nc.tensor.matmul(
                                ps_scores[b * NODES:(b + 1) * NODES, c * HC:(c + 1) * HC, :],
                                qT[:, gpar, c, n0:n0 + NODES], k_diag[:, par, c, b, :, :], start=True, stop=True)
                    last.then_inc(scores_done, 1)
                if has_pair(r, O_LAG):
                    if r == O_LAG:
                        pe.wait_ge(w_lo_ready, 4 * CH)
                    pe.wait_ge(oT_lo_ready, s - O_LAG + 1)
                    wait(pe, y_ready, s - O_LAG)
                    split_matmuls(ps_out[:], lambda c: (oT_hi[:, c, :], oT_lo[:, c, :]),
                                  lambda c: (w_hi["o"][:, c, :], w_lo["o"][:, c, :])).then_inc(projected, 1)
                if has_pair(r, T_LAG):
                    wait_apart(pe, probsT_ready, s - T_LAG + 1)
                    wait_apart(pe, v_ready, s - T_LAG + 1)
                    wait_apart(pe, oT_ready, s - T_LAG)
                    for h in range(HEADS):
                        quad, c = h % HC, h // HC
                        for b in range(2):
                            k = slice(b * NODES, (b + 1) * NODES)
                            last = nc.tensor.matmul(
                                ps_oT[quad * DH:(quad + 1) * DH, b, c, :],
                                v_sb[k, 1 - par, h * DH:(h + 1) * DH], probsT[k, h, :], start=True, stop=True)
                    last.then_inc(attended, 1)
                if r < PAIRS:
                    if r and r % GP == 0:
                        pe.wait_ge(x_lo_ready, s + GP)
                    for i in range(2):
                        wait(pe, qk_out[i], s)
                        project_qk(s, r, i)

            steps(pe, step)


_INS = ["x", "adj", "L0_gnn_Wq", "L0_gnn_bq", "L0_gnn_Wk", "L0_gnn_bk",
        "L0_gnn_Wv", "L0_gnn_bv", "L0_gnn_Wo", "L0_gnn_bo"]


def kernel(**inputs):
    import numpy as np
    import concourse.bacc as bacc
    from concourse.bass_utils import run_bass_kernel_spmd

    nc = bacc.Bacc("TRN2", target_bir_lowering=False, num_devices=1)
    x = np.asarray(inputs["x"])
    arrays = {"in_xT": np.ascontiguousarray(x.reshape(-1, x.shape[-1]).T)}
    for name in _INS:
        arrays[f"in_{name}"] = np.ascontiguousarray(inputs[name])
    aps = [nc.dram_tensor(k, a.shape, mybir.dt.from_np(a.dtype), kind="ExternalInput").ap()
           for k, a in arrays.items()]
    out = nc.dram_tensor("out", x.shape, mybir.dt.float32, kind="ExternalOutput").ap()
    graph_attention_layernorm(nc, *aps, out)
    r = run_bass_kernel_spmd(nc, [arrays], core_ids=[0])
    return r.results[0]["out"]
```

```python
import concourse.bass as bass
from concourse import mybir
from contextlib import ExitStack


def graph_attention_layernorm(nc, xT, adjP, bias_cols, identity_in, x, Wq, Wk, Wv, Wo, bo, out):
    F32 = mybir.dt.float32
    F32R = mybir.dt.float32r
    I32 = mybir.dt.int32
    ALU = mybir.AluOpType
    ACT = mybir.ActivationFunctionType
    AX = mybir.AxisListType

    BATCHES, NODES, D = x.shape
    HEADS = 16
    DH = D // HEADS
    P = 128
    CH = D // P
    HC = P // DH
    PAIRS = BATCHES // 2
    GP = 4
    GN = GP * P
    SCALE = float(DH) ** -0.5
    NEG = -1.0e30
    EPS = 1e-5

    V_LAG, S_LAG, T_LAG = 3, 4, 5
    O_LAG, N_LAG = 6, 7
    AHEAD = 4
    STEPS = PAIRS + N_LAG
    LAST_S, LAST_T, LAST_O = (PAIRS - 1 + lag for lag in (S_LAG, T_LAG, O_LAG))
    RB = 4
    VB = 4
    TURN = 8
    LOOP_END = PAIRS - TURN
    HALVES = ((0, CH // 2), (CH // 2, CH))

    x_v = x.rearrange("b n d -> (b n) d")
    out_v = out.rearrange("b n d -> (b n) d")

    ctx = ExitStack()
    with ctx:
        def sb(name, shape, dt=F32):
            return ctx.enter_context(nc.sbuf_tensor(name, shape, dt))

        def pb(name, shape):
            return ctx.enter_context(nc.psum_tensor(name, shape, F32))

        def sem(name):
            return ctx.enter_context(nc.semaphore(name))

        w_hi = {n: sb(f"w{n}_hi", [P, CH, D], F32R) for n in "qkvo"}
        w_lo = {n: sb(f"w{n}_lo", [P, CH, D], F32R) for n in "qkvo"}
        w_stage = sb("w_stage", [P, 2, CH, D])
        x_raw = sb("x_raw", [P, 2, CH, P])
        x_hi = sb("x_hi", [P, 2, CH, GN], F32R)
        x_lo = sb("x_lo", [P, 2, CH, GN], F32R)
        qT = sb("qT", [P, 2, CH, GN])
        kT = sb("kT", [P, 2, CH, GN])
        v_sb = sb("v_sb", [P, VB, D])
        k_diag = sb("k_diag", [P, 2, CH, 2, HC, NODES])
        scores = sb("scores", [P, 2, HEADS, NODES])
        probsT = sb("probsT", [P, HEADS, 2, NODES])
        oT = sb("oT", [P, CH, 2, NODES])
        oT_hi = sb("oT_hi", [P, CH, P], F32R)
        oT_lo = sb("oT_lo", [P, CH, P], F32R)
        resid = sb("resid", [P, RB, D])
        bo_rows = sb("bo_rows", [P, D])
        biases = sb("biases", [P, 3, CH])
        bq_col, bk_col, bv_col = (biases[:, i, :] for i in range(3))
        adj_sb = sb("adj_sb", [P, GP, NODES], I32)
        no_edge = sb("no_edge", [P, GP, NODES])
        row_max = sb("row_max", [P, 2, HEADS])
        row_sum = sb("row_sum", [P, 2, HEADS])
        row_inv = sb("row_inv", [P, 2, HEADS])
        stats = sb("stats", [P, nc.vector.BN_STATS_DIM])
        mean_var = sb("mean_var", [P, 2, 2])
        var_eps = sb("var_eps", [P, 1])
        rstd = sb("rstd", [P, 2])
        minus_half = sb("minus_half", [P, 1])
        identity = sb("identity", [P, P])

        ps_v = pb("ps_v", [P, D])
        ps_qk = [pb(f"ps_qk{i}", [P, GN]) for i in range(2)]
        ps_out = [pb(f"ps_out{i}", [P, D]) for i in range(2)]
        ps_scores = pb("ps_scores", [P, HEADS, NODES])
        ps_oT = pb("ps_oT", [P, CH, 2, NODES])

        x_first_in = [sem(f"x_first_in{c}") for c in range(CH)]
        wq_in = [sem(f"wq_in{c}") for c in range(CH)]
        weights_in = {n: sem(f"weights_in_{n}") for n in "kvo"}
        biases_in = sem("biases_in")
        identity_loaded = sem("identity_loaded")
        bo_in = sem("bo_in")
        x_raw_in = [sem(f"x_raw_in{i}") for i in range(2)]
        adj_in = sem("adj_in")
        resid_in = [sem(f"resid_in{i}") for i in range(RB)]
        stored = [sem(f"stored{i}") for i in range(RB)]
        half_ready = sem("half_ready")
        k_diag_zero = sem("k_diag_zero")
        probsT_zero = sem("probsT_zero")
        w_hi_ready = sem("w_hi_ready")
        w_vo_hi_ready = sem("w_vo_hi_ready")
        w_lo_ready = sem("w_lo_ready")
        x_hi_ready = sem("x_hi_ready")
        x_lo_ready = sem("x_lo_ready")
        v_done = sem("v_done")
        v_ready = sem("v_ready")
        qk_done = [sem(f"qk{i}_done") for i in range(2)]
        qk_out = [sem(f"qk{i}_out") for i in range(2)]
        k_diag_ready = sem("k_diag_ready")
        scores_done = sem("scores_done")
        no_edge_ready = sem("no_edge_ready")
        scores_masked = sem("scores_masked")
        max_ready = sem("max_ready")
        shifted = sem("shifted")
        exp_ready = sem("exp_ready")
        sum_ready = sem("sum_ready")
        inv_ready = sem("inv_ready")
        probs_ready = sem("probs_ready")
        last_probs_ready = sem("last_probs_ready")
        probsT_ready = sem("probsT_ready")
        attended = sem("attended")
        oT_ready = sem("oT_ready")
        oT_hi_ready = sem("oT_hi_ready")
        oT_lo_ready = sem("oT_lo_ready")
        oT_part_ready = sem("oT_part_ready")
        oT_hi_part_ready = sem("oT_hi_part_ready")
        oT_lo_part_ready = sem("oT_lo_part_ready")
        oT_lo_last_ready = sem("oT_lo_last_ready")
        projected = sem("projected")
        resid_biased = sem("resid_biased")
        y_ready = sem("y_ready")
        stats_ready = sem("stats_ready")
        mean_var_ready = sem("mean_var_ready")
        var_eps_ready = sem("var_eps_ready")
        rstd_ready = sem("rstd_ready")
        normed = sem("normed")
        waits_passed = {e: sem(f"waits_passed{i}") for i, e in enumerate((nc.gpsimd, nc.vector))}

        block = ctx.enter_context(nc.Block())

        def steps(engine, step):
            for s in range(TURN):
                step(s, s)
            with engine.Fori(1, LOOP_END // TURN) as turn:
                for j in range(TURN):
                    step(turn * TURN + j, TURN + j)
            for s in range(LOOP_END, STEPS):
                step(s, s)

        def has_pair(r, lag):
            return 0 <= r - lag < PAIRS

        def wait(engine, semaphore, value):
            if not isinstance(value, int) or value > 0:
                engine.wait_ge(semaphore, value)

        def wait_apart(engine, semaphore, value):
            wait(engine, semaphore, value)
            if not isinstance(value, int):
                engine.sem_inc(waits_passed[engine], 1)

        def qk_chunk(r, i):
            u = 2 * (r % GP) + i
            return "qk"[u // CH], u % CH

        x_first = scores[:].rearrange("p a h k -> p (a h k)").rearrange("p (c n) -> p c n", n=GN)
        staged = {"q": qT[:, 1], "k": kT[:, 1], "v": w_stage[:, 0], "o": w_stage[:, 1]}

        @block.sync
        def _(sp):
            def load_x(s, r):
                sp.dma_start(x_raw[:, r % 2], xT[:, bass.ds(s, 1)].rearrange("p t c n -> p (t c) n")
                             ).then_inc(x_raw_in[r % 2], 16)

            for c in range(CH):
                sp.dma_start(x_first[:, c, :].rearrange("p (t n) -> p t n", n=P), xT[:, 0:GP, c, :]).then_inc(x_first_in[c], 16)
                sp.dma_start(staged["q"][:, c, :], Wq[c * P:(c + 1) * P, :]).then_inc(wq_in[c], 16)
            sp.dma_start(biases[:], bias_cols).then_inc(biases_in, 16)
            for t in range(AHEAD, AHEAD + 2):
                load_x(t, t)
            sp.dma_start(staged["k"], Wk.rearrange("(c p) n -> p c n", p=P)).then_inc(weights_in["k"], 16)
            sp.dma_start(bo_rows[:], bo.partition_broadcast(P)).then_inc(bo_in, 16)
            for n, w in (("v", Wv), ("o", Wo)):
                sp.dma_start(staged[n], w.rearrange("(c p) n -> p c n", p=P)).then_inc(weights_in[n], 16)
            sp.dma_start(adj_sb[:], adjP[:, 0:GP, :]).then_inc(adj_in, 16)
            sp.dma_start(identity[:], identity_in).then_inc(identity_loaded, 16)

            def step(s, r):
                if r % GP == 0 and has_pair(r, S_LAG) and r < PAIRS:
                    sp.wait_ge(scores_masked, s - S_LAG + 1)
                    sp.dma_start(adj_sb[:], adjP[:, bass.ds(s, GP), :]).then_inc(adj_in, 16)
                if r + AHEAD + 2 < PAIRS:
                    sp.wait_ge(x_lo_ready, s + AHEAD + 1)
                    load_x(s + AHEAD + 2, r)
                if r < RB:
                    sp.dma_start(resid[:, r, :], x_v[r * P:(r + 1) * P, :]).then_inc(resid_in[r], 16)
                if has_pair(r, N_LAG):
                    buf = (r - N_LAG) % RB
                    sp.wait_ge(normed, s - N_LAG + 1)
                    sp.dma_start(out_v[bass.ds((s - N_LAG) * P, P), :],
                                 resid[:, buf, :]).then_inc(stored[buf], 16)
                    if has_pair(r + RB, N_LAG):
                        sp.wait_ge(stored[buf], (s - N_LAG - buf) * (16 // RB) + 16)
                        sp.dma_start(resid[:, buf, :],
                                     x_v[bass.ds((s - N_LAG + RB) * P, P), :]).then_inc(resid_in[buf], 16)

            steps(sp, step)
            for i in range(RB):
                sp.wait_ge(stored[i], 16 * (PAIRS // RB))

        @block.gpsimd
        def _(pool):
            nc.gpsimd.memset(minus_half[:], -0.5).then_inc(half_ready, 1)
            for c in range(CH):
                pool.wait_ge(x_hi_ready, c + 1)
                nc.gpsimd.tensor_tensor(x_lo[:, 0, c, :], x_first[:, c, :], x_hi[:, 0, c, :].bitcast(F32),
                                        ALU.subtract).then_inc(x_lo_ready, 1)
            nc.gpsimd.memset(k_diag[:], 0.0).then_inc(k_diag_zero, 1)
            nc.gpsimd.memset(probsT[:], 0.0).then_inc(probsT_zero, 1)
            pool.wait_ge(bo_in, 16)
            pool.wait_ge(half_ready, 1)

            def inverse_deviation(s, r):
                par = r % 2
                pool.wait_ge(var_eps_ready, s - O_LAG + 1)
                nc.gpsimd.tensor_tensor(rstd[:, par:par + 1], var_eps[:], minus_half[:],
                                        ALU.pow).then_inc(rstd_ready, 1)

            def step(s, r):
                par = r % 2
                if PAIRS <= r < LAST_O:
                    for i, (c0, c1) in enumerate(HALVES):
                        pool.wait_ge(oT_hi_part_ready, 2 * (s - PAIRS) + i + 1)
                        nc.gpsimd.tensor_tensor(oT_lo[:, c0:c1], oT[:, c0:c1].rearrange("p c b q -> p c (b q)"),
                                                oT_hi[:, c0:c1].bitcast(F32),
                                                ALU.subtract).then_inc(oT_lo_part_ready, 1)
                elif r < PAIRS and has_pair(r, O_LAG):
                    pool.wait_ge(oT_hi_ready, s - O_LAG + 1)
                    nc.gpsimd.tensor_tensor(oT_lo[:], oT[:].rearrange("p c b q -> p c (b q)"),
                                            oT_hi[:].bitcast(F32), ALU.subtract).then_inc(oT_lo_ready, 1)
                if r + AHEAD < PAIRS:
                    gpar, n = (r // GP + 1) % 2, slice(r % GP * P, (r % GP + 1) * P)
                    pool.wait_ge(x_hi_ready, s + AHEAD + 1)
                    nc.gpsimd.tensor_tensor(x_lo[:, gpar, :, n], x_raw[:, par], x_hi[:, gpar, :, n].bitcast(F32),
                                            ALU.subtract).then_inc(x_lo_ready, 1)
                if has_pair(r, S_LAG):
                    pool.wait_ge(max_ready, s - S_LAG + 1)
                    nc.gpsimd.tensor_tensor(scores[:, par], scores[:, par],
                                            row_max[:, par, :].unsqueeze(2).to_broadcast([P, HEADS, NODES]),
                                            ALU.subtract).then_inc(shifted, 1)
                if has_pair(r, T_LAG):
                    buf = (r - T_LAG) % RB
                    pool.wait_ge(resid_in[buf], (s - T_LAG - buf) * (16 // RB) + 16)
                    nc.gpsimd.tensor_tensor(resid[:, buf, :], resid[:, buf, :], bo_rows[:],
                                            ALU.add).then_inc(resid_biased, 1)
                if r == LAST_S + 1:
                    inverse_deviation(LAST_S, LAST_S)
                if has_pair(r, S_LAG) and r != LAST_S:
                    pool.wait_ge(inv_ready, s - S_LAG + 1)
                    nc.gpsimd.tensor_tensor(scores[:, par], scores[:, par],
                                            row_inv[:, par, :].unsqueeze(2).to_broadcast([P, HEADS, NODES]),
                                            ALU.mult).then_inc(probs_ready, 1)
                if has_pair(r, O_LAG) and r != LAST_S:
                    inverse_deviation(s, r)

            steps(pool, step)

        @block.scalar
        def _(act):
            for c in range(CH):
                act.wait_ge(x_first_in[c], 16)
                nc.scalar.copy(x_hi[:, 0, c, :], x_first[:, c, :]).then_inc(x_hi_ready, 1)
                act.wait_ge(wq_in[c], 16)
                nc.scalar.copy(w_hi["q"][:, c, :], staged["q"][:, c, :]).then_inc(w_hi_ready, 1)
            act.wait_ge(biases_in, 16)

            def qk_to_sbuf(s, r, i):
                gpar = (r // GP) % 2
                kind, m = qk_chunk(r, i)
                dst, bias = (qT, bq_col) if kind == "q" else (kT, bk_col)
                act.wait_ge(qk_done[i], s + 1)
                nc.scalar.activation(dst[:, gpar, m, :], ps_qk[i][:], ACT.Identity,
                                     bias=bias[:, m:m + 1]).then_inc(qk_out[i], 1)

            def spread_keys(s, r):
                par, gpar, j = r % 2, ((r - S_LAG) // GP) % 2, r % GP
                if j == 0:
                    act.wait_ge(qk_out[1], s)
                if r == S_LAG:
                    act.wait_ge(k_diag_zero, 1)
                wait(act, scores_done, s - S_LAG - 1)
                for h in range(HC):
                    q = slice(h * DH, (h + 1) * DH)
                    last = nc.scalar.copy(
                        k_diag[q, par, :, :, h, :],
                        kT[q, gpar, :, j * P:(j + 1) * P].rearrange("p c (b k) -> p c b k", b=2))
                last.then_inc(k_diag_ready, 1)

            def step(s, r):
                par = r % 2
                if r == 1:
                    act.wait_ge(weights_in["k"], 16)
                    for c in range(CH):
                        nc.scalar.copy(w_hi["k"][:, c, :], staged["k"][:, c, :]).then_inc(w_hi_ready, 1)
                if has_pair(r, S_LAG):
                    act.wait_ge(v_done, s - S_LAG + 1)
                    wait(act, attended, s - S_LAG - VB + 1)
                    nc.scalar.copy(v_sb[:, (r - S_LAG) % VB, :], ps_v[:]).then_inc(v_ready, 1)
                if r >= PAIRS and has_pair(r, O_LAG):
                    act.wait_ge(attended, s - O_LAG + 1)
                    for i, (c0, c1) in enumerate(HALVES):
                        for c in range(c0, c1):
                            last = nc.scalar.activation(oT[:, c], ps_oT[:, c], ACT.Identity, bias=bv_col[:, c:c + 1])
                        last.then_inc(oT_part_ready, 1)
                        act.wait_ge(oT_part_ready, 2 * (s - PAIRS) + i + 1)
                        nc.scalar.copy(oT_hi[:, c0:c1], oT[:, c0:c1].rearrange("p c b q -> p c (b q)")
                                       ).then_inc(oT_hi_part_ready, 1)
                if r < PAIRS and has_pair(r, O_LAG):
                    act.wait_ge(oT_ready, s - O_LAG + 1)
                    nc.scalar.copy(oT_hi[:], oT[:].rearrange("p c b q -> p c (b q)")).then_inc(oT_hi_ready, 1)
                if r + AHEAD < PAIRS:
                    gpar, n = (r // GP + 1) % 2, slice(r % GP * P, (r % GP + 1) * P)
                    act.wait_ge(x_raw_in[par], (s - par) * 8 + 16)
                    nc.scalar.copy(x_hi[:, gpar, :, n], x_raw[:, par]).then_inc(x_hi_ready, 1)
                if has_pair(r + 1, S_LAG) and (r + 1) % GP != 0:
                    spread_keys(s + 1, r + 1)
                if r < PAIRS:
                    qk_to_sbuf(s, r, 0)
                if has_pair(r, S_LAG):
                    act.wait_ge(shifted, s - S_LAG + 1)
                    nc.scalar.activation(scores[:, par], scores[:, par], ACT.Exp, scale=SCALE).then_inc(exp_ready, 1)
                if r < PAIRS:
                    qk_to_sbuf(s, r, 1)
                if has_pair(r + 1, S_LAG) and (r + 1) % GP == 0:
                    spread_keys(s + 1, r + 1)

            steps(act, step)

        @block.vector
        def _(dve):
            for i, n in enumerate("qkvo"):
                if n == "k":
                    dve.wait_ge(weights_in["k"], 16)
                if n in "vo":
                    dve.wait_ge(weights_in[n], 16)
                    for c in range(CH):
                        nc.vector.tensor_copy(w_hi[n][:, c, :], staged[n][:, c, :]).then_inc(w_vo_hi_ready, 1)
                for c in range(CH):
                    if n in "qk":
                        dve.wait_ge(w_hi_ready, CH * i + c + 1)
                    else:
                        dve.wait_ge(w_vo_hi_ready, CH * (i - 2) + c + 1)
                    nc.vector.tensor_tensor(w_lo[n][:, c, :], staged[n][:, c, :], w_hi[n][:, c, :].bitcast(F32),
                                            ALU.subtract).then_inc(w_lo_ready, 1)
            dve.wait_ge(biases_in, 16)

            def transpose_probs(s, r):
                if r == T_LAG:
                    dve.wait_ge(probsT_zero, 1)
                if r >= PAIRS:
                    dve.wait_ge(attended, s - T_LAG)
                if r == LAST_T:
                    dve.wait_ge(last_probs_ready, 1)
                else:
                    dve.wait_ge(probs_ready, s - T_LAG + 1)
                for b in range(2):
                    for qh in range(2):
                        for kh in range(2):
                            src, dst = b * NODES + qh * DH, b * NODES + kh * DH
                            last = nc.vector.transpose(
                                probsT[dst:dst + DH, :, b, qh * DH:(qh + 1) * DH],
                                scores[src:src + DH, (r - T_LAG) % 2, :, kh * DH:(kh + 1) * DH])
                last.then_inc(probsT_ready, 1)

            def step(s, r):
                par = r % 2
                if r < PAIRS and has_pair(r, O_LAG):
                    dve.wait_ge(attended, s - O_LAG + 1)
                    nc.vector.tensor_tensor(oT[:], ps_oT[:],
                                            bv_col.unsqueeze(2).unsqueeze(3).to_broadcast([P, CH, 2, NODES]),
                                            ALU.add).then_inc(oT_ready, 1)
                if r == LAST_O:
                    for i, (c0, c1) in enumerate(HALVES):
                        dve.wait_ge(oT_hi_part_ready, 2 * (s - PAIRS) + i + 1)
                        nc.vector.tensor_tensor(oT_lo[:, c0:c1], oT[:, c0:c1].rearrange("p c b q -> p c (b q)"),
                                                oT_hi[:, c0:c1].bitcast(F32),
                                                ALU.subtract).then_inc(oT_lo_last_ready, 1)
                if has_pair(r, S_LAG):
                    j = r % GP
                    if j == 0:
                        dve.wait_ge(adj_in, (s - S_LAG) * 4 + 16)
                        nc.vector.tensor_scalar(no_edge[:], adj_sb[:], 0, NEG, ALU.is_equal,
                                                ALU.mult).then_inc(no_edge_ready, 1)
                        dve.wait_ge(no_edge_ready, s // GP)
                    dve.wait_ge(scores_done, s - S_LAG + 1)
                    nc.vector.tensor_tensor(scores[:, par], ps_scores[:],
                                            no_edge[:, j:j + 1, :].to_broadcast([P, HEADS, NODES]),
                                            ALU.add).then_inc(scores_masked, 1)
                    dve.wait_ge(scores_masked, s - S_LAG + 1)
                    nc.vector.reduce_max(row_max[:, par, :], scores[:, par], AX.X).then_inc(max_ready, 1)
                if has_pair(r, N_LAG):
                    dve.wait_ge(rstd_ready, s - N_LAG + 1)
                    buf = (r - N_LAG) % RB
                    y = ps_out[1 - par][:] if r - N_LAG + O_LAG >= PAIRS else resid[:, buf, :]
                    nc.vector.tensor_scalar(resid[:, buf, :], y, mean_var[:, 1 - par, 0:1],
                                            rstd[:, 1 - par:2 - par], ALU.subtract, ALU.mult).then_inc(normed, 1)
                if has_pair(r, T_LAG) and r != LAST_T:
                    transpose_probs(s, r)
                if has_pair(r, S_LAG):
                    dve.wait_ge(exp_ready, s - S_LAG + 1)
                    nc.vector.reduce_sum(row_sum[:, par, :], scores[:, par], AX.X).then_inc(sum_ready, 1)
                    dve.wait_ge(sum_ready, s - S_LAG + 1)
                    nc.vector.reciprocal(row_inv[:, par, :], row_sum[:, par, :]).then_inc(inv_ready, 1)
                if r == LAST_S:
                    dve.wait_ge(inv_ready, PAIRS)
                    nc.vector.tensor_tensor(scores[:, par], scores[:, par],
                                            row_inv[:, par, :].unsqueeze(2).to_broadcast([P, HEADS, NODES]),
                                            ALU.mult).then_inc(last_probs_ready, 1)
                    transpose_probs(LAST_T, LAST_T)
                if has_pair(r, O_LAG):
                    buf = (r - O_LAG) % RB
                    dve.wait_ge(projected, s - O_LAG + 1)
                    if r < PAIRS:
                        dve.wait_ge(resid_biased, s - O_LAG + 1)
                        nc.vector.tensor_tensor(resid[:, buf, :], ps_out[par][:], resid[:, buf, :],
                                                ALU.add).then_inc(y_ready, 1)
                        dve.wait_ge(y_ready, s - O_LAG + 1)
                        nc.vector.bn_stats(stats[:], resid[:, buf, :]).then_inc(stats_ready, 1)
                    else:
                        nc.vector.bn_stats(stats[:], ps_out[par][:]).then_inc(stats_ready, 1)
                    wait_apart(dve, stats_ready, s - O_LAG + 1)
                    nc.vector.bn_aggr(mean_var[:, par, :], stats[:]).then_inc(mean_var_ready, 1)
                    dve.wait_ge(mean_var_ready, s - O_LAG + 1)
                    nc.vector.tensor_scalar(var_eps[:], mean_var[:, par, 1:2], EPS, None,
                                            ALU.add).then_inc(var_eps_ready, 1)

            steps(dve, step)

        @block.tensor
        def _(pe):
            def split_matmuls(dst, lhs, rhs, ready=lambda c: None, start=True):
                for c in range(CH):
                    ready(c)
                    (l_hi, l_lo), (r_hi, r_lo) = lhs(c), rhs(c)
                    nc.tensor.matmul(dst, l_hi, r_hi, start=start and c == 0, stop=False)
                    nc.tensor.matmul(dst, l_hi, r_lo, start=False, stop=False)
                    last = nc.tensor.matmul(dst, l_lo, r_hi, start=False, stop=(c == CH - 1))
                return last

            def project_qk(s, r, i):
                gpar = (r // GP) % 2
                kind, m = qk_chunk(r, i)
                cols = slice(m * P, (m + 1) * P)

                def ready(c):
                    if kind == "q" and r < GP:
                        pe.wait_ge(w_lo_ready, c + 1)
                        pe.wait_ge(x_lo_ready, c + 1)
                    if kind == "k" and r < GP:
                        pe.wait_ge(w_lo_ready, CH + c + 1)

                split_matmuls(ps_qk[i][:], lambda c: (w_hi[kind][:, c, cols], w_lo[kind][:, c, cols]),
                              lambda c: (x_hi[:, gpar, c, :], x_lo[:, gpar, c, :]), ready).then_inc(qk_done[i], 1)

            def step(s, r):
                par = r % 2

                def score(lag):
                    gpar, j = ((r - lag) // GP) % 2, (r - lag) % GP
                    pe.wait_ge(k_diag_ready, s - lag + 1)
                    wait(pe, scores_masked, s - lag)
                    for c in range(CH):
                        for b in range(2):
                            n0 = j * P + b * NODES
                            last = nc.tensor.matmul(
                                ps_scores[b * NODES:(b + 1) * NODES, c * HC:(c + 1) * HC, :],
                                qT[:, gpar, c, n0:n0 + NODES], k_diag[:, (r - lag) % 2, c, b, :, :],
                                start=True, stop=True)
                    last.then_inc(scores_done, 1)

                def project_out():
                    def ready(c):
                        if r < PAIRS and c == 0:
                            pe.wait_ge(oT_lo_ready, s - O_LAG + 1)
                        if r >= PAIRS and c * 2 % CH == 0:
                            if r < LAST_O:
                                pe.wait_ge(oT_lo_part_ready, 2 * (s - PAIRS) + c * 2 // CH + 1)
                            else:
                                pe.wait_ge(oT_lo_last_ready, c * 2 // CH + 1)

                    if r == O_LAG:
                        pe.wait_ge(w_lo_ready, 4 * CH)
                    if r < PAIRS + 2:
                        wait(pe, y_ready, s - O_LAG - 1)
                    else:
                        pe.wait_ge(normed, s - O_LAG - 1)
                    if r >= PAIRS:
                        pe.wait_ge(identity_loaded, 16)
                        pe.wait_ge(resid_biased, s - O_LAG + 1)
                        nc.tensor.matmul(ps_out[par][:], identity[:], resid[:, (r - O_LAG) % RB, :],
                                         start=True, stop=False)
                    split_matmuls(ps_out[par][:], lambda c: (oT_hi[:, c, :], oT_lo[:, c, :]),
                                  lambda c: (w_hi["o"][:, c, :], w_lo["o"][:, c, :]), ready,
                                  start=r < PAIRS).then_inc(projected, 1)

                def project_v():
                    gpar, j = ((r - V_LAG) // GP) % 2, (r - V_LAG) % GP
                    if r == V_LAG:
                        pe.wait_ge(w_lo_ready, 3 * CH)
                    wait(pe, v_ready, s - V_LAG)
                    n = slice(j * P, (j + 1) * P)
                    split_matmuls(ps_v[:], lambda c: (x_hi[:, gpar, c, n], x_lo[:, gpar, c, n]),
                                  lambda c: (w_hi["v"][:, c, :], w_lo["v"][:, c, :])).then_inc(v_done, 1)

                if has_pair(r, S_LAG) and r <= PAIRS:
                    score(S_LAG)
                if r < PAIRS:
                    if r and r % GP == 0:
                        pe.wait_ge(x_lo_ready, s + GP)
                    wait(pe, qk_out[0], s)
                    project_qk(s, r, 0)
                elif has_pair(r, V_LAG):
                    project_v()
                if has_pair(r, O_LAG):
                    project_out()
                if r >= PAIRS and has_pair(r + 1, S_LAG):
                    score(S_LAG - 1)
                if r < PAIRS:
                    wait(pe, qk_out[1], s)
                    project_qk(s, r, 1)
                    if has_pair(r, V_LAG):
                        project_v()
                if has_pair(r, T_LAG):
                    pe.wait_ge(probsT_ready, s - T_LAG + 1)
                    pe.wait_ge(v_ready, s - T_LAG + 1)
                    if r < PAIRS:
                        wait(pe, oT_ready, s - T_LAG)
                    else:
                        pe.wait_ge(oT_part_ready, 2 * (s - PAIRS + 1))
                    for h in range(HEADS):
                        quad, c = h % HC, h // HC
                        last = nc.tensor.matmul(ps_oT[quad * DH:(quad + 1) * DH, c, :, :],
                                                v_sb[:, (r - T_LAG) % VB, h * DH:(h + 1) * DH], probsT[:, h, :, :],
                                                start=True, stop=True)
                    last.then_inc(attended, 1)

            steps(pe, step)


_P, _PAIR = 128, 2


def kernel(**inputs):
    import numpy as np
    import concourse.bacc as bacc
    from concourse.bass_utils import run_bass_kernel_spmd

    nc = bacc.Bacc("TRN2", target_bir_lowering=False, num_devices=1)
    x, adj = np.asarray(inputs["x"]), np.asarray(inputs["adj"])
    batches, nodes, d = x.shape
    pairs = batches // _PAIR
    arrays = {
        "in_xT": np.ascontiguousarray(x.reshape(pairs, _P, d // _P, _P).transpose(3, 0, 2, 1)),
        "in_adj": np.ascontiguousarray(adj.reshape(pairs, _P, nodes).transpose(1, 0, 2)),
        "in_bias_cols": np.ascontiguousarray(np.stack(
            [np.asarray(inputs[f"L0_gnn_b{n}"]).reshape(d // _P, _P) for n in "qkv"]).transpose(2, 0, 1)),
        "in_identity": np.eye(_P, dtype=np.float32),
        "in_x": np.ascontiguousarray(x),
    }
    for name in ("Wq", "Wk", "Wv", "Wo", "bo"):
        arrays[f"in_{name}"] = np.ascontiguousarray(inputs[f"L0_gnn_{name}"])
    aps = [nc.dram_tensor(k, a.shape, mybir.dt.from_np(a.dtype), kind="ExternalInput").ap()
           for k, a in arrays.items()]
    out = nc.dram_tensor("out", x.shape, mybir.dt.float32, kind="ExternalOutput").ap()
    graph_attention_layernorm(nc, *aps, out)
    r = run_bass_kernel_spmd(nc, [arrays], core_ids=[0])
    return r.results[0]["out"]
```
